# Optimizing a Trainium2 kernel written in Bass

```python
import numpy as np
import jax
import jax.numpy as jnp

def _softmax(x, axis=-1):
    return jax.nn.softmax(x, axis=axis)
def _gelu(x):
    return jax.nn.gelu(x, approximate=True)
def _silu(x):
    return jax.nn.silu(x)
def _sigmoid(x):
    return jax.nn.sigmoid(x)
def _layernorm(x, axis=-1, eps=1e-5):
    m = jnp.mean(x, axis=axis, keepdims=True)
    v = jnp.var(x, axis=axis, keepdims=True)
    return (x - m) / jnp.sqrt(v + eps)
def _scatter_add(tgt, idx, src, axis=0):
    return tgt.at[idx].add(src)
def _segment_sum(src, seg, n):
    return jax.ops.segment_sum(src, seg, n)

kernel_name = 'mk_conv_seq_d1_conv_nchw32_0fd8ea'

def setup_inputs(seed: int = 0):
    np.random.seed(seed)
    _w = jnp.asarray
    def _rec_inputs():
        import jax
        import jax.numpy as jnp
        _gk = jax.random.key(seed)
        x = -7.109e-05 + 0.9999 * jax.random.normal(jax.random.fold_in(_gk, 1), (8, 32, 512, 512), jnp.float32)
        return x
    x = _rec_inputs()
    def _L0_conv_setup():
        import jax, jax.numpy as jnp
        import numpy as np
        from jax import lax
        B, CIN, COUT, H, W, K, KS = (8, 32, 32, 512, 512, 4, 3)
        EPS = 1e-05
        key = jax.random.key(seed)
        ks = jax.random.split(key, 4)
        x = jax.random.normal(ks[0], (B, CIN, H, W), jnp.float32)
        kernels = jax.random.normal(ks[1], (K, COUT, CIN, KS, KS), jnp.float32) * 0.05
        w_att = jax.random.normal(ks[2], (K, CIN), jnp.float32) * 0.1
        b_att = jax.random.normal(ks[3], (K,), jnp.float32) * 0.01
        gamma = jnp.ones((COUT,), jnp.float32)
        beta = jnp.zeros((COUT,), jnp.float32)
        return {'x': x, 'kernels': kernels, 'w_att': w_att, 'b_att': b_att, 'gamma': gamma, 'beta': beta}
    _L0_conv_all = _L0_conv_setup()
    _L0_conv_in = {k: v for k, v in _L0_conv_all.items() if k in ('kernels', 'w_att', 'b_att', 'gamma', 'beta', )}
    del _L0_conv_all

    return {
        "x": x,
        "L0_conv_kernels": _L0_conv_in["kernels"],
        "L0_conv_w_att": _L0_conv_in["w_att"],
        "L0_conv_b_att": _L0_conv_in["b_att"],
        "L0_conv_gamma": _L0_conv_in["gamma"],
        "L0_conv_beta": _L0_conv_in["beta"],
    }

def reference(x, L0_conv_kernels, L0_conv_w_att, L0_conv_b_att, L0_conv_gamma, L0_conv_beta):
    import jax
    import jax.numpy as jnp
    def _L0_conv_ref(x, kernels, w_att, b_att, gamma, beta):
        import jax, jax.numpy as jnp
        import numpy as np
        from jax import lax
        B, CIN, COUT, H, W, K, KS = (8, 32, 32, 512, 512, 4, 3)
        EPS = 1e-05
        pooled = x.mean(axis=(2, 3))
        att = jax.nn.softmax(pooled @ w_att.T + b_att, axis=1)
        k_comb = jnp.einsum('bk,koiuv->boiuv', att, kernels)

        def conv_one(xi, wi):
            return lax.conv_general_dilated(xi[None], wi, window_strides=(1, 1), padding='SAME', dimension_numbers=('NCHW', 'OIHW', 'NCHW'))[0]
        out = jax.vmap(conv_one)(x, k_comb)
        mean = out.mean(axis=(0, 2, 3))
        var = out.var(axis=(0, 2, 3))
        scale = (gamma * lax.rsqrt(var + EPS))[None, :, None, None]
        out = (out - mean[None, :, None, None]) * scale + beta[None, :, None, None]
        return jnp.maximum(out, 0.0)

    def _gn(v, G=16, eps=1e-5):
        B_, C_, H_, W_ = v.shape
        g = v.reshape(B_, G, C_ // G, H_, W_)
        m = jnp.mean(g, axis=(2, 3, 4), keepdims=True)
        s = jnp.var(g, axis=(2, 3, 4), keepdims=True)
        return ((g - m) / jnp.sqrt(s + eps)).reshape(v.shape)

    def _ln_c(v, eps=1e-6):
        m = jnp.mean(v, axis=1, keepdims=True)
        s = jnp.var(v, axis=1, keepdims=True)
        return (v - m) / jnp.sqrt(s + eps)

    def _ln_t(v, eps=1e-5):
        m = jnp.mean(v, axis=-1, keepdims=True)
        s = jnp.var(v, axis=-1, keepdims=True)
        return (v - m) / jnp.sqrt(s + eps)

    def _to_tokens(v):
        B_, C_, H_, W_ = v.shape
        return v.reshape(B_, C_, H_ * W_).transpose(0, 2, 1)
    def _from_tokens(t, like):
        B_, C_, H_, W_ = like.shape
        return t.transpose(0, 2, 1).reshape(B_, C_, H_, W_)

    x = _L0_conv_ref(x, L0_conv_kernels, L0_conv_w_att, L0_conv_b_att, L0_conv_gamma, L0_conv_beta)
    return x


_drawn_inputs = setup_inputs


def setup_inputs(seed=0):
    import zlib

    import numpy as np

    out = dict(_drawn_inputs(seed))
    spreads = {'L0_conv_gamma': (1.0, 0.2), 'L0_conv_beta': (0.0, 0.1)}
    factors = {'L0_conv_w_att': 56.985, 'L0_conv_b_att': 4.224}
    for name, (base, spread) in spreads.items():
        noise = np.random.default_rng([zlib.crc32(name.encode()), seed]).standard_normal(out[name].shape)
        drawn = base * np.exp(spread * noise) if base else spread * noise
        out[name] = jnp.asarray(drawn.astype(out[name].dtype))
    for name, factor in factors.items():
        out[name] = (out[name] * factor).astype(out[name].dtype)
    return out
```

```python
from contextlib import ExitStack

import concourse.bass as bass
from concourse import mybir

ALU = mybir.AluOpType
ACT = mybir.ActivationFunctionType
AX_X = mybir.AxisListType.X
F32 = mybir.dt.float32
F32R = mybir.dt.float32r

P = 128
EPS = 1e-5


def dynamic_conv_batchnorm_relu(
    nc: bass.Bass,
    x: bass.AP,
    kernels: bass.AP,
    w_att: bass.AP,
    b_att: bass.AP,
    gamma: bass.AP,
    beta: bass.AP,
    out: bass.AP,
):
    B, CI, H, W = x.shape
    K, CO, _, KS, _ = kernels.shape
    assert (CI, CO, KS) == (32, 32, 3) and K * CO == P
    TAPS = KS + 1
    X = W // 2
    WIN = 8
    TILES = H // (2 * WIN)
    PAIRS = 2
    G = P // CI
    ROW = 2 * (X + 3)
    ODD = X + 3
    FLAT = H * W // P
    BANK = 512
    CHUNKS = TILES * 4
    PIXELS = B * H * W
    RING2 = 4

    assert TILES % 2 == 0 and CI == TILES

    with ExitStack() as ctx:
        def sb(name, shape, dt=F32):
            return ctx.enter_context(nc.sbuf_tensor(name, shape, dt))

        def sem(name):
            return ctx.enter_context(nc.semaphore(name))

        raw = nc.dram_tensor("raw_conv", [B * TILES, CO, G, WIN, X], F32, kind="Internal").ap()

        arena = sb("arena", [P, 8, FLAT])
        x_tile = arena[:, 0:4, :].rearrange("p a n -> p (a n)").rearrange("p (s w c) -> p s w c", s=2, w=WIN)
        raw_tile = arena[:, 4:6, :].rearrange("p s (w c) -> p s w c", w=WIN)
        pool_tile = arena[:, 6:8, :]
        read_tile = arena[:, 0:4, :].rearrange("p s (r f j c) -> p s r f j c", r=2, f=2, j=2)
        norm_tile = arena[:, 4:8, :].rearrange("p s (j r c f) -> p s f r j c", j=2, r=2, f=2)

        head = sb("head", [P, 2, WIN, ROW], F32R)
        rest = sb("rest", [P, 2, WIN, ROW], F32R)
        w_head = sb("w_head", [P, TAPS, P], F32R)
        w_rest = sb("w_rest", [P, TAPS, P], F32R)
        w_sum = sb("w_sum", [P, TAPS * P])
        w_each = sb("w_each", [P, K, TAPS, CO, 2, 2])
        k_rows = sb("k_rows", [P, 2, KS, CI, G])
        k_raw = sb("k_raw", [P, CI, KS, KS])
        ident = sb("ident", [P, P])
        ones = sb("ones", [P, P])
        same_channel = sb("same_channel", [P, CO, G])
        zeros = sb("zeros", [CI, W])
        sums = sb("sums", [P, CI])
        pooled = sb("pooled", [P, CI])
        watt = sb("watt", [P, K, CI])
        batt = sb("batt", [P, K])
        prod = sb("prod", [P, K, CI])
        logit = sb("logit", [P, K])
        small = sb("small", [P, 4])
        expo = sb("expo", [P, K])
        att = sb("att", [P, K])
        stats = sb("stats", [P, CHUNKS, 6])
        triples = sb("triples", [P, B, 3])
        count = sb("count", [P, 1])
        sample_mv = sb("sample_mv", [P, 2])
        total = sb("total", [P, 2])
        fin = sb("fin", [P, 12])
        gam = sb("gam", [P, 1])
        bet = sb("bet", [P, 1])
        scale = sb("scale", [P, 1])
        shift = sb("shift", [P, 1])
        ps = ctx.enter_context(nc.psum_tensor("ps", [P, 8, BANK], F32))

        params_loaded = sem("params_loaded")
        kernels_loaded = sem("kernels_loaded")
        x_loaded = [sem(f"x_loaded{i}") for i in range(2)]
        pool_loaded = [sem(f"pool_loaded{i}") for i in range(2)]
        raw_written = [sem(f"raw_written{i}") for i in range(2)]
        read_loaded = [sem(f"read_loaded{i}") for i in range(RING2)]
        out_written = [sem(f"out_written{i}") for i in range(RING2)]
        pool_summed = sem("pool_summed")
        zeros_set = sem("zeros_set")
        consts_set = sem("consts_set")
        sel_cleared = sem("sel_cleared")
        k_rows_set = sem("k_rows_set")
        taps_turned = sem("taps_turned")
        w_each_done = sem("w_each_done")
        pool_total = sem("pool_total")
        pool_total_read = sem("pool_total_read")
        logits_ready = sem("logits_ready")
        exp_ready = sem("exp_ready")
        weights_ready = sem("weights_ready")
        att_chain = sem("att_chain")
        head_ready = sem("head_ready")
        rest_ready = sem("rest_ready")
        pair_done = sem("pair_done")
        raw_copied = sem("raw_copied")
        stats_done = sem("stats_done")
        aggr_done = sem("aggr_done")
        fin_chain = sem("fin_chain")
        mean_ready = sem("mean_ready")
        var_ready = sem("var_ready")
        dev_ready = sem("dev_ready")
        meansum_ready = sem("meansum_ready")
        varsum_ready = sem("varsum_ready")
        sqrt_ready = sem("sqrt_ready")
        scale_ready = sem("scale_ready")
        normalised = sem("normalised")

        ATT_STEPS = 6 + K

        def tiles_of_sample(eng, b, step):
            step(b, 0, 0)
            step(b, 1, 1)
            with eng.Fori(1, TILES // 2 - 1) as j:
                step(b, 2 * j, 0)
                step(b, 2 * j + 1, 1)
            step(b, TILES - 2, 0)
            step(b, TILES - 1, 1)

        def all_samples(eng, sample):
            sample(0)
            with eng.Fori(1, B - 1) as b:
                sample(b)
            sample(B - 1)

        def fixed(v):
            return isinstance(v, int)

        block = ctx.enter_context(nc.Block())

        @block.sync
        def _(sp):
            sp.dma_start(k_raw[:, :, :, :], kernels.rearrange("k o i u v -> (k o) i u v")).then_inc(kernels_loaded, 16)

            def load_pool(b, c, slot):
                src = x[bass.ds(b, 1), bass.ds(c, 1), :, :].rearrange("b c (p h) w -> (b c p) (h w)", p=P)
                sp.dma_start(pool_tile[:, slot, :], src).then_inc(pool_loaded[slot], 16)

            load_pool(0, 0, 0)
            load_pool(0, 1, 1)
            sp.dma_start(watt[:, :, :], w_att.partition_broadcast(P)).then_inc(params_loaded, 16)
            sp.dma_start(batt[:, :], b_att.partition_broadcast(P)).then_inc(params_loaded, 16)
            for g in range(G):
                for t, v in ((gam, gamma), (bet, beta)):
                    sp.dma_start(t[g:P:G, :], v.rearrange("(c o) -> c o", o=1)).then_inc(params_loaded, 16)

            def load_x(b, t, slot):
                top, bottom = fixed(t) and t == 0, fixed(t) and t == TILES - 1
                for g in range(G):
                    part = x_tile[g:P:G, slot, :, :]
                    cuts = [(0, WIN)]
                    if bottom and g == G - 1:
                        cuts = [(0, WIN - 1), (WIN - 1, WIN)]
                    if not bottom and g == 0:
                        cuts = [(0, 1), (1, WIN)]
                    for w0, w1 in cuts:
                        if (top and g == 0 and w0 == 0) or (bottom and w0 == WIN - 1):
                            src = zeros[:, :].unsqueeze(1)
                        else:
                            row = 2 * WIN * t + 2 * w0 - 1 + g
                            odd = row % 2 if fixed(row) else (g + 1) % 2
                            src = x[bass.ds(b, 1), :, bass.ds(row - odd, 2 * (w1 - w0)), :]
                            src = src.rearrange("b c (w o) x -> (b c) w o x", o=2)[:, :, odd, :]
                        sp.dma_start(part[:, w0:w1, :], src).then_inc(x_loaded[slot], 16)

            with sp.Fori(0, CI // 2 - 1) as c2:
                for slot in range(2):
                    sp.wait_ge(pool_summed, 2 * c2 + slot + 1)
                    load_pool(0, 2 * c2 + 2 + slot, slot)

            def step(b, t, slot):
                n = TILES * b + t
                if fixed(n) and n == 0:
                    sp.wait_ge(zeros_set, 1)
                if not fixed(n) or n >= 2:
                    sp.wait_ge(rest_ready, n - 1)
                load_x(b, t, slot)
                if fixed(b) and b == B - 1:
                    return
                if fixed(t) and t == TILES - 1:
                    return
                first = fixed(t) and t == 0
                for c, s in ([(0, 0), (1, 1)] if first else [(t + 1, (slot + 1) % 2)]):
                    sp.wait_ge(pool_summed, CI * (b + 1) + c - 1)
                    load_pool(b + 1, c, s)

            all_samples(sp, lambda b: tiles_of_sample(sp, b, step))

            def read(n, slot):
                for jb in range(G):
                    src = raw[bass.ds(n, 1), :, :, 2 * jb:2 * jb + 2, :].rearrange("n o q j x -> (n o) q (j x)")
                    dst = read_tile[jb:P:G, slot, :, :, :, :].rearrange("p r f j x -> p (r f) (j x)")
                    sp.dma_start(dst, src).then_inc(read_loaded[slot], 16)

            def write(b, t, slot):
                dst = out[bass.ds(b, 1), :, bass.ds(2 * WIN * t, 2 * WIN), :]
                dst = dst.rearrange("b c (q r) x -> (b c) q (r x)", q=G)
                sp.dma_start(dst, arena[:, 4 + slot, :]).then_inc(out_written[slot], 16)

            for s in range(2):
                sp.wait_ge(raw_written[s], 16 * B * TILES // 2)
            sp.wait_ge(raw_copied, PAIRS * B * TILES)
            for s in range(RING2):
                read(s, s)
            def ring(b, u, more):
                for s in range(RING2):
                    n = TILES * b + RING2 * u + s
                    sp.wait_ge(normalised, 2 * n + 2)
                    if more:
                        read(n + RING2, s)
                    write(b, RING2 * u + s, s)

            with sp.Fori(0, B - 1) as b:
                with sp.Fori(0, TILES // RING2) as u:
                    ring(b, u, True)
            with sp.Fori(0, TILES // RING2 - 1) as u:
                ring(B - 1, u, True)
            ring(B - 1, TILES // RING2 - 1, False)
            for s in range(RING2):
                sp.wait_ge(out_written[s], 16 * B * TILES // RING2)

        @block.gpsimd
        def _(pool):
            nc.gpsimd.memset(zeros[:, :], 0.0).then_inc(zeros_set, 1)
            nc.gpsimd.memset(ident[:, :], 0.0).then_inc(sel_cleared, 1)
            nc.gpsimd.memset(same_channel[:, :, :], 0.0).then_inc(sel_cleared, 1)
            nc.gpsimd.memset(ones[:, :], 1.0).then_inc(consts_set, 1)
            pool.wait_ge(sel_cleared, 2)
            nc.gpsimd.affine_select(out=ident[:, :], in_=ident[:, :], compare_op=ALU.not_equal, fill=1.0,
                                    base=0, pattern=[[-1, P]], channel_multiplier=1).then_inc(consts_set, 1)
            for off in range(G):
                pool.wait_ge(sel_cleared, 2 + off)
                nc.gpsimd.affine_select(out=same_channel[:, :, :], in_=same_channel[:, :, :],
                                        compare_op=ALU.not_equal, fill=1.0 / G, base=-off,
                                        pattern=[[-G, CO], [0, G]],
                                        channel_multiplier=1).then_inc(sel_cleared, 1)

        def split_view(t, slot):
            return t[:, slot, :, :].rearrange("p w (f c) -> p w f c", f=2)[:, :, :, 0:X]

        def x_view(slot):
            return x_tile[:, slot, :, :].rearrange("p w (c f) -> p w f c", f=2)

        @block.scalar
        def _(act):
            def sum_channel(b, c, slot):
                act.wait_ge(pool_loaded[slot], 8 * (CI * b + c - slot) + 16)
                nc.scalar.activation(pool_tile[:, slot, :], pool_tile[:, slot, :], ACT.Copy,
                                     accum_out=sums[:, bass.ds(c, 1)]).then_inc(pool_summed, 1)

            def exponentials(b):
                act.wait_ge(logits_ready, b + 1)
                nc.scalar.activation(expo[:, :], logit[:, :], ACT.Exp, bias=small[:, 0:1],
                                     accum_out=small[:, 1:2]).then_inc(exp_ready, 1)

            def split_head(b, t, slot):
                act.wait_ge(x_loaded[slot], 40 * (TILES * b + t - slot) + 80)
                nc.scalar.activation(split_view(head, slot), x_view(slot), ACT.Copy).then_inc(head_ready, 1)

            def copy_pair(n, half, slot):
                act.wait_ge(pair_done, PAIRS * n + half + 1)
                bank = 4 * slot + 2 * half
                nc.scalar.activation(raw_tile[:, slot, 4 * half:4 * half + 4, :].rearrange("p w c -> p (w c)"),
                                     ps[:, bank:bank + 2, :].rearrange("p a n -> p (a n)"),
                                     ACT.Copy).then_inc(raw_copied, 1)

            def write_raw(n, slot):
                act.wait_ge(raw_copied, PAIRS * n + PAIRS)
                dst = raw[bass.ds(n, 1), :, :, :, :].rearrange("n o q w x -> (n o q) w x")
                act.dma_start(dst, raw_tile[:, slot, :, :]).then_inc(raw_written[slot], 16)

            with act.Fori(0, CI // 2) as c2:
                for slot in range(2):
                    sum_channel(0, 2 * c2 + slot, slot)
            exponentials(0)
            split_head(0, 0, 0)

            def step(b, t, slot):
                n = TILES * b + t
                other = 1 - slot
                if not fixed(n) or n >= 1:
                    copy_pair(n - 1, 1, other)
                    write_raw(n - 1, other)
                last = fixed(n) and n == B * TILES - 1
                if not last:
                    if fixed(t) and t == TILES - 1:
                        split_head(b + 1, 0, other)
                    else:
                        split_head(b, t + 1, other)
                if not (fixed(b) and b == B - 1):
                    if fixed(t) and t == 0:
                        act.wait_ge(pool_total, b + 1)
                        sum_channel(b + 1, 0, 0)
                        sum_channel(b + 1, 1, 1)
                    elif fixed(t) and t == TILES - 1:
                        exponentials(b + 1)
                    else:
                        sum_channel(b + 1, t + 1, other)
                if not fixed(n) or n >= 2:
                    act.wait_ge(raw_written[slot], 8 * (n - slot))
                    act.wait_ge(stats_done, PAIRS * n - 2)
                copy_pair(n, 0, slot)

            all_samples(act, lambda b: tiles_of_sample(act, b, step))
            copy_pair(B * TILES - 1, 1, 1)
            write_raw(B * TILES - 1, 1)

            act.wait_ge(varsum_ready, 1)
            nc.scalar.activation(fin[:, 3:4], fin[:, 2:3], ACT.Sqrt).then_inc(sqrt_ready, 1)
            act.wait_ge(scale_ready, 1)
            def normalise(u):
                for s in range(RING2):
                    act.wait_ge(read_loaded[s], 64 * u + 64)
                    if not fixed(u):
                        act.wait_ge(out_written[s], 16 * u)
                    for f in range(2):
                        nc.scalar.activation(norm_tile[:, s, f, :, :, :], read_tile[:, s, :, f, :, :], ACT.Relu,
                                             bias=shift[:, 0:1], scale=scale[:, 0:1]).then_inc(normalised, 1)

            normalise(0)
            with act.Fori(1, B * TILES // RING2) as u:
                normalise(u)

        @block.vector
        def _(dve):
            for t in (head, rest):
                nc.vector.memset(t[:, :, :, X:ODD].bitcast(F32), 0.0).then_inc(k_rows_set, 1)
            nc.vector.memset(w_each[:, :, :, :, :, :], 0.0).then_inc(k_rows_set, 1)
            nc.vector.memset(k_rows[:, :, :, :, :], 0.0).then_inc(k_rows_set, 1)
            nc.vector.memset(triples[:, :, :], float(H * W // G)).then_inc(k_rows_set, 1)
            dve.wait_ge(kernels_loaded, 16)
            dve.wait_ge(k_rows_set, 4)
            for ro in range(2):
                nc.vector.tensor_copy(k_rows[:, ro, :, :, ro:ro + KS],
                                      k_raw[:, :, :, :].rearrange("p i u v -> p v i u")).then_inc(k_rows_set, 1)
            dve.wait_ge(taps_turned, 1)
            for ro in range(2):
                for dx in range(KS):
                    i = ro * KS + dx
                    turned = ps[:, i // 4, (i % 4) * P:(i % 4 + 1) * P].rearrange("p (k o) -> p k o", k=K)
                    for f in range(2):
                        last = nc.vector.tensor_copy(w_each[:, :, dx + f, :, ro, f], turned)
            last.then_inc(w_each_done, 1)

            def attention(b):
                k0 = ATT_STEPS * b
                dve.wait_ge(pool_total, b + 1)
                nc.vector.tensor_scalar(pooled[:, :], ps[:, 7, 0:CI], 1.0 / (H * W), None,
                                        ALU.mult).then_inc(pool_total_read, 1)
                dve.wait_ge(pool_total_read, b + 1)
                nc.vector.tensor_tensor(prod[:, :, :], watt[:, :, :],
                                        pooled[:, :].unsqueeze(1).to_broadcast([P, K, CI]),
                                        ALU.mult).then_inc(att_chain, 1)
                dve.wait_ge(att_chain, k0 + 1)
                nc.vector.tensor_reduce(logit[:, :], prod[:, :, :], AX_X, ALU.add).then_inc(att_chain, 1)
                dve.wait_ge(att_chain, k0 + 2)
                nc.vector.tensor_tensor(logit[:, :], logit[:, :], batt[:, :], ALU.add).then_inc(att_chain, 1)
                dve.wait_ge(att_chain, k0 + 3)
                nc.vector.tensor_reduce(small[:, 2:3], logit[:, :], AX_X, ALU.max).then_inc(att_chain, 1)
                dve.wait_ge(att_chain, k0 + 4)
                nc.vector.tensor_scalar(small[:, 0:1], small[:, 2:3], -1.0, None, ALU.mult).then_inc(logits_ready, 1)

            def combine(b):
                k0 = ATT_STEPS * b
                dve.wait_ge(exp_ready, b + 1)
                nc.vector.reciprocal(small[:, 3:4], small[:, 1:2]).then_inc(att_chain, 1)
                dve.wait_ge(att_chain, k0 + 5)
                nc.vector.tensor_scalar(att[:, :], expo[:, :], small[:, 3:4], None, ALU.mult).then_inc(att_chain, 1)
                dve.wait_ge(att_chain, k0 + 6)
                for k in range(K):
                    one = w_each[:, k, :, :, :, :].rearrange("p s o r f -> p (s o r f)")
                    if k == 0:
                        last = nc.vector.tensor_scalar(w_sum[:, :], one, att[:, 0:1], None, ALU.mult)
                    else:
                        last = nc.vector.scalar_tensor_tensor(out=w_sum[:, :], in0=one, scalar=att[:, k:k + 1],
                                                              in1=w_sum[:, :], op0=ALU.mult, op1=ALU.add)
                    last.then_inc(att_chain, 1)
                    dve.wait_ge(att_chain, k0 + 7 + k)

            def split_weights(b):
                flat = w_head[:, :, :].rearrange("p s m -> p (s m)")
                if not fixed(b) or b > 0:
                    dve.wait_ge(pair_done, PAIRS * TILES * b)
                nc.vector.tensor_copy(flat, w_sum[:, :]).then_inc(weights_ready, 1)
                dve.wait_ge(weights_ready, 2 * b + 1)
                nc.vector.tensor_tensor(w_rest[:, :, :].rearrange("p s m -> p (s m)"), w_sum[:, :],
                                        flat.bitcast(F32), ALU.subtract).then_inc(weights_ready, 1)

            def split_rest(n, slot):
                dve.wait_ge(head_ready, n + 1)
                nc.vector.tensor_tensor(split_view(rest, slot), x_view(slot), split_view(head, slot).bitcast(F32),
                                        ALU.subtract).then_inc(rest_ready, 1)

            def pair_stats(n, t, half, slot):
                dve.wait_ge(raw_copied, PAIRS * n + half + 1)
                for a in range(2):
                    last = nc.vector.bn_stats(stats[:, bass.ds(4 * t + 2 * half + a, 1), :].rearrange("p o s -> p (o s)"),
                                              raw_tile[:, slot, 4 * half + 2 * a:4 * half + 2 * a + 2, :]
                                              .rearrange("p w c -> p (w c)"))
                last.then_inc(stats_done, 1)

            def aggregate(b):
                dve.wait_ge(stats_done, PAIRS * TILES * (b + 1))
                nc.vector.memset(count[:, :], float(H * W // G))
                nc.vector.bn_aggr(sample_mv[:, :], stats[:, :, :].rearrange("p c s -> p (c s)")).then_inc(aggr_done, 1)
                dve.wait_ge(aggr_done, 3 * b + 1)
                one = triples[:, bass.ds(b, 1), :].rearrange("p o s -> p (o s)")
                nc.vector.tensor_copy(one[:, 1:2], sample_mv[:, 0:1]).then_inc(aggr_done, 1)
                nc.vector.tensor_scalar(one[:, 2:3], sample_mv[:, 1:2], float(H * W // G), None,
                                        ALU.mult).then_inc(aggr_done, 1)
                dve.wait_ge(aggr_done, 3 * b + 3)

            dve.wait_ge(params_loaded, 16 * 10)
            attention(0)
            combine(0)
            split_weights(0)
            split_rest(0, 0)

            def step(b, t, slot):
                n = TILES * b + t
                other = 1 - slot
                last_sample = fixed(b) and b == B - 1
                final = fixed(t) and t == TILES - 1
                if final and not last_sample:
                    attention(b + 1)
                if fixed(t) and t == 0:
                    if not fixed(b) or b > 0:
                        pair_stats(n - 1, TILES - 1, 1, other)
                        aggregate(b - 1)
                else:
                    pair_stats(n - 1, t - 1, 1, other)
                if not (final and last_sample):
                    split_rest(n + 1, other)
                if final and not last_sample:
                    combine(b + 1)
                pair_stats(n, t, 0, slot)
                if final and not last_sample:
                    split_weights(b + 1)

            all_samples(dve, lambda b: tiles_of_sample(dve, b, step))
            pair_stats(B * TILES - 1, TILES - 1, 1, 1)
            aggregate(B - 1)

            chain = [0]

            def link(ins):
                chain[0] += 1
                ins.then_inc(fin_chain, 1)
                dve.wait_ge(fin_chain, chain[0])

            nc.vector.bn_aggr(total[:, :], triples[:, :, :].rearrange("p b s -> p (b s)")).then_inc(mean_ready, 1)
            dve.wait_ge(meansum_ready, 1)
            link(nc.vector.tensor_copy(fin[:, 0:1], ps[:, 0, 0:1]))
            link(nc.vector.tensor_tensor(fin[:, 4:5], total[:, 0:1], fin[:, 0:1], ALU.subtract))
            link(nc.vector.tensor_tensor(fin[:, 5:6], fin[:, 4:5], fin[:, 4:5], ALU.mult))
            nc.vector.tensor_tensor(fin[:, 1:2], fin[:, 5:6], total[:, 1:2], ALU.add).then_inc(dev_ready, 1)
            dve.wait_ge(var_ready, 1)
            nc.vector.tensor_scalar(fin[:, 2:3], ps[:, 1, 0:1], EPS, None, ALU.add).then_inc(varsum_ready, 1)
            dve.wait_ge(sqrt_ready, 1)
            link(nc.vector.reciprocal(fin[:, 6:7], fin[:, 3:4]))
            link(nc.vector.tensor_tensor(fin[:, 7:8], fin[:, 6:7], fin[:, 6:7], ALU.mult))
            link(nc.vector.tensor_tensor(fin[:, 8:9], fin[:, 7:8], fin[:, 2:3], ALU.mult))
            link(nc.vector.tensor_scalar(fin[:, 9:10], fin[:, 8:9], -0.5, 1.5, ALU.mult, ALU.add))
            link(nc.vector.tensor_tensor(fin[:, 10:11], fin[:, 9:10], fin[:, 6:7], ALU.mult))
            link(nc.vector.tensor_tensor(scale[:, :], fin[:, 10:11], gam[:, :], ALU.mult))
            link(nc.vector.tensor_tensor(fin[:, 11:12], scale[:, :], fin[:, 0:1], ALU.mult))
            nc.vector.tensor_tensor(shift[:, :], bet[:, :], fin[:, 11:12], ALU.subtract).then_inc(scale_ready, 1)

        @block.tensor
        def _(pe):
            pe.wait_ge(k_rows_set, 7)
            pe.wait_ge(consts_set, 2)
            for ro in range(2):
                for dx in range(KS):
                    i = ro * KS + dx
                    rows = k_rows[:, ro, dx, :, :].rearrange("p i g -> p (i g)")
                    last = nc.tensor.matmul(ps[:, i // 4, (i % 4) * P:(i % 4 + 1) * P], rows, ident[:, :],
                                            start=True, stop=True)
            last.then_inc(taps_turned, 1)

            def total_pool(b):
                pe.wait_ge(pool_summed, CI * (b + 1))
                nc.tensor.matmul(ps[:, 7, 0:CI], ones[:, :], sums[:, :], start=True, stop=True).then_inc(pool_total, 1)

            total_pool(0)

            def step(b, t, slot):
                n = TILES * b + t
                if not fixed(n) or n >= 2:
                    pe.wait_ge(raw_copied, PAIRS * n - 2)
                if fixed(t) and t == 0:
                    pe.wait_ge(weights_ready, 2 * b + 2)
                last_tile = fixed(t) and t == TILES - 1
                if last_tile and not (fixed(b) and b == B - 1):
                    total_pool(b + 1)
                if fixed(n) and n == 1:
                    pe.wait_ge(pool_total_read, 1)
                pe.wait_ge(head_ready, n + 1)
                for bank in range(4):
                    if bank == 3 and last_tile and not (fixed(b) and b == B - 1):
                        pe.wait_ge(pool_total_read, b + 2)
                    for i, (w, part) in enumerate(((w_head, head), (w_rest, head), (w_head, rest))):
                        if i == 2 and bank == 0:
                            pe.wait_ge(rest_ready, n + 1)
                        for s in range(TAPS):
                            at = (ODD - 1, 0, ODD, 1)[s]
                            last = nc.tensor.matmul(ps[:, 4 * slot + bank, :], w[:, s, :],
                                                    part[:, slot, 2 * bank:2 * bank + 2, at:at + X],
                                                    start=(i == 0 and s == 0), stop=(i == 2 and s == TAPS - 1))
                    if bank % 2:
                        last.then_inc(pair_done, 1)

            all_samples(pe, lambda b: tiles_of_sample(pe, b, step))

            pe.wait_ge(sel_cleared, 6)
            pe.wait_ge(mean_ready, 1)
            pe.wait_ge(raw_copied, PAIRS * B * TILES)
            sel = same_channel[:, :, :].rearrange("p c g -> p (c g)")
            nc.tensor.matmul(ps[:, 0, 0:1], sel, total[:, 0:1], start=True, stop=True).then_inc(meansum_ready, 1)
            pe.wait_ge(dev_ready, 1)
            nc.tensor.matmul(ps[:, 1, 0:1], sel, fin[:, 1:2], start=True, stop=True).then_inc(var_ready, 1)


_INS = ['x', 'L0_conv_kernels', 'L0_conv_w_att', 'L0_conv_b_att', 'L0_conv_gamma', 'L0_conv_beta']


def kernel(**inputs):
    import numpy as _np
    import concourse.bacc as _bacc
    from concourse import mybir as _mybir
    from concourse.bass_utils import run_bass_kernel_spmd as _run

    nc = _bacc.Bacc("TRN2", target_bir_lowering=False, num_devices=1)
    arrays, args = {}, []
    for name in _INS:
        a = _np.ascontiguousarray(inputs[name])
        arrays[f"in_{name}_dram"] = a
        args.append(nc.dram_tensor(f"in_{name}_dram", a.shape, _mybir.dt.from_np(a.dtype), kind="ExternalInput").ap())
    shape = inputs['x'].shape[:1] + (inputs['L0_conv_kernels'].shape[1],) + inputs['x'].shape[2:]
    args.append(nc.dram_tensor("out_dram", shape, _mybir.dt.float32, kind="ExternalOutput").ap())
    dynamic_conv_batchnorm_relu(nc, *args)
    r = _run(nc, [arrays], core_ids=[0])
    return r.results[0]["out_dram"]
```

```python
from contextlib import ExitStack

import concourse.bass as bass
from concourse import mybir

ALU = mybir.AluOpType
ACT = mybir.ActivationFunctionType
AX_X = mybir.AxisListType.X
F32 = mybir.dt.float32
F32R = mybir.dt.float32r

P = 128
EPS = 1e-5


def dynamic_conv_batchnorm_relu(
    nc: bass.Bass,
    x: bass.AP,
    kernels: bass.AP,
    w_att: bass.AP,
    b_att: bass.AP,
    gamma: bass.AP,
    beta: bass.AP,
    out: bass.AP,
):
    B, CI, H, W = x.shape
    K, CO, _, KS, _ = kernels.shape
    assert (CI, CO, KS) == (32, 32, 3) and K * CO == P
    TAPS = KS + 1
    X = W // 2
    WIN = 8
    TILES = H // (2 * WIN)
    LOADED = WIN // 2 + 1
    PAIRS = 2
    G = P // CI
    ROW = 2 * (X + 3)
    ODD = X + 3
    FLAT = H * W // P
    BANK = 512
    CHUNKS = TILES * 4
    PIXELS = B * H * W
    RING2 = 4

    assert TILES % 2 == 0 and CI == TILES

    with ExitStack() as ctx:
        def sb(name, shape, dt=F32):
            return ctx.enter_context(nc.sbuf_tensor(name, shape, dt))

        def sem(name):
            return ctx.enter_context(nc.semaphore(name))

        raw = nc.dram_tensor("raw_conv", [B * TILES, CO, G, WIN, X], F32, kind="Internal").ap()

        arena = sb("arena", [P, 4, FLAT])
        raw_tile = arena[:, 0:2, :].rearrange("p s (w c) -> p s w c", w=WIN)
        norm_tile = arena[:, :, :].rearrange("p s (j r c f) -> p s f r j c", j=2, r=2, f=2)
        x_tile = sb("x_tile", [P, 2, LOADED, W])
        read_tile = sb("read_tile", [P, RING2, 2, 2, 2, X])

        head = sb("head", [P, 2, WIN + 1, ROW], F32R)
        rest = sb("rest", [P, 2, WIN + 1, ROW], F32R)
        w_head = sb("w_head", [P, TAPS, P], F32R)
        w_rest = sb("w_rest", [P, TAPS, P], F32R)
        w_sum = sb("w_sum", [P, TAPS * P])
        w_each = sb("w_each", [P, K, TAPS, CO, 2, 2])
        k_rows = sb("k_rows", [P, 2, KS, G, CI])
        k_raw = sb("k_raw", [P, CI, KS, KS])
        ident = sb("ident", [P, P])
        ones = sb("ones", [P, P])
        same_channel = sb("same_channel", [P, CO, G])
        zeros = sb("zeros", [CI, W])
        sums = sb("sums", [P, CI])
        pooled = sb("pooled", [P, CI])
        watt = sb("watt", [P, K, CI])
        batt = sb("batt", [P, K])
        prod = sb("prod", [P, K, CI])
        logit = sb("logit", [P, K])
        small = sb("small", [P, 4])
        expo = sb("expo", [P, K])
        att = sb("att", [P, K])
        stats = sb("stats", [P, CHUNKS, 6])
        triples = sb("triples", [P, B, 3])
        count = sb("count", [P, 1])
        sample_mv = sb("sample_mv", [P, 2])
        total = sb("total", [P, 2])
        fin = sb("fin", [P, 12])
        gam = sb("gam", [P, 1])
        bet = sb("bet", [P, 1])
        scale = sb("scale", [P, 1])
        shift = sb("shift", [P, 1])
        ps = ctx.enter_context(nc.psum_tensor("ps", [P, 8, BANK], F32))

        params_loaded = sem("params_loaded")
        kernels_loaded = sem("kernels_loaded")
        first_loaded = [sem(f"first_loaded{i}") for i in range(4)]
        x_loaded = [sem(f"x_loaded{i}") for i in range(2)]
        pool_loaded = [sem(f"pool_loaded{i}") for i in range(2)]
        raw_written = [sem(f"raw_written{i}") for i in range(2)]
        read_loaded = [sem(f"read_loaded{i}") for i in range(RING2)]
        out_written = [sem(f"out_written{i}") for i in range(RING2)]
        pool_summed = sem("pool_summed")
        zeros_set = sem("zeros_set")
        consts_set = sem("consts_set")
        sel_cleared = sem("sel_cleared")
        k_rows_set = sem("k_rows_set")
        taps_turned = sem("taps_turned")
        w_each_done = sem("w_each_done")
        pool_total = sem("pool_total")
        pool_total_read = sem("pool_total_read")
        logits_ready = sem("logits_ready")
        exp_ready = sem("exp_ready")
        weights_ready = sem("weights_ready")
        att_chain = sem("att_chain")
        head_ready = sem("head_ready")
        rest_ready = sem("rest_ready")
        odd_head_low_ready = sem("odd_head_low_ready")
        odd_head_up_ready = sem("odd_head_up_ready")
        odd_rest_ready = sem("odd_rest_ready")
        pair_done = sem("pair_done")
        raw_copied = sem("raw_copied")
        stats_done = sem("stats_done")
        aggr_done = sem("aggr_done")
        fin_chain = sem("fin_chain")
        mean_ready = sem("mean_ready")
        var_ready = sem("var_ready")
        dev_ready = sem("dev_ready")
        meansum_ready = sem("meansum_ready")
        varsum_ready = sem("varsum_ready")
        sqrt_ready = sem("sqrt_ready")
        scale_ready = sem("scale_ready")
        normalised = sem("normalised")

        ATT_STEPS = 6 + K

        def tiles_of_sample(eng, b, step):
            step(b, 0, 0)
            step(b, 1, 1)
            with eng.Fori(1, TILES // 2 - 1) as j:
                step(b, 2 * j, 0)
                step(b, 2 * j + 1, 1)
            step(b, TILES - 2, 0)
            step(b, TILES - 1, 1)

        def all_samples(eng, sample):
            sample(0)
            with eng.Fori(1, B - 1) as b:
                sample(b)
            sample(B - 1)

        def fixed(v):
            return isinstance(v, int)

        block = ctx.enter_context(nc.Block())

        @block.sync
        def _(sp):
            sp.dma_start(k_raw[:, :, :, :], kernels.rearrange("k o i u v -> (k o) i u v")).then_inc(kernels_loaded, 16)

            def load_channel(b, c, slot, signal):
                src = x[bass.ds(b, 1), bass.ds(c, 1), :, :].rearrange("b c (p h) w -> (b c p) (h w)", p=P)
                sp.dma_start(arena[:, slot, :], src).then_inc(signal, 16)

            for c in range(4):
                load_channel(0, c, c, first_loaded[c])
            sp.dma_start(watt[:, :, :], w_att.partition_broadcast(P)).then_inc(params_loaded, 16)
            sp.dma_start(batt[:, :], b_att.partition_broadcast(P)).then_inc(params_loaded, 16)
            for g in range(G):
                for t, v in ((gam, gamma), (bet, beta)):
                    sp.dma_start(t[g:P:G, :], v.rearrange("(c o) -> c o", o=1)).then_inc(params_loaded, 16)

            def load_x(b, t, slot):
                top, bottom = fixed(t) and t == 0, fixed(t) and t == TILES - 1
                for g in range(G):
                    cuts = [(0, LOADED if g < 2 else LOADED - 1)]
                    if bottom and g == 1:
                        cuts = [(0, LOADED - 1), (LOADED - 1, LOADED)]
                    if not bottom and g == 0:
                        cuts = [(0, 1), (1, LOADED)]
                    for v0, v1 in cuts:
                        dst = x_tile[g * CI:(g + 1) * CI, slot, v0:v1, :]
                        if (top and g == 0 and v0 == 0) or (bottom and g == 1 and v0 == LOADED - 1):
                            src = zeros[:, :].unsqueeze(1)
                        else:
                            at = 2 * WIN * t + 4 * v0 - (4 if g == 0 else 0)
                            src = x[bass.ds(b, 1), :, bass.ds(at, 4 * (v1 - v0)), :]
                            src = src.rearrange("b c (v o) x -> (b c) v o x", o=4)[:, :, (g - 1) % 4, :]
                        sp.dma_start(dst, src).then_inc(x_loaded[slot], 16)

            with sp.Fori(1, CI // 4) as u:
                for s in range(4):
                    sp.wait_ge(pool_summed, 4 * u + s - 3)
                    load_channel(0, 4 * u + s, s, first_loaded[s])

            def step(b, t, slot):
                n = TILES * b + t
                if fixed(n) and n == 0:
                    sp.wait_ge(zeros_set, 2)
                if not fixed(n) or n >= 2:
                    sp.wait_ge(rest_ready, n - 1)
                load_x(b, t, slot)
                if fixed(b) and b == B - 1:
                    return
                if fixed(t) and t == TILES - 1:
                    return
                first = fixed(t) and t == 0
                for c, s in ([(0, 0), (1, 1)] if first else [(t + 1, (slot + 1) % 2)]):
                    sp.wait_ge(pool_summed, CI * (b + 1) + c - 1)
                    load_channel(b + 1, c, 2 + s, pool_loaded[s])

            all_samples(sp, lambda b: tiles_of_sample(sp, b, step))

            def read(n, slot):
                for jb in range(G):
                    src = raw[bass.ds(n, 1), :, :, 2 * jb:2 * jb + 2, :].rearrange("n o q j x -> (n o) q (j x)")
                    dst = read_tile[jb:P:G, slot, :, :, :, :].rearrange("p r f j x -> p (r f) (j x)")
                    sp.dma_start(dst, src).then_inc(read_loaded[slot], 16)

            def write(b, t, slot):
                dst = out[bass.ds(b, 1), :, bass.ds(2 * WIN * t, 2 * WIN), :]
                dst = dst.rearrange("b c (q r) x -> (b c) q (r x)", q=G)
                sp.dma_start(dst, arena[:, slot, :]).then_inc(out_written[slot], 16)

            for s in range(2):
                sp.wait_ge(raw_written[s], 16 * RING2 // 2)
            for s in range(RING2):
                read(s, s)
            for s in range(2):
                sp.wait_ge(raw_written[s], 16 * B * TILES // 2)
            def ring(b, u, more):
                for s in range(RING2):
                    n = TILES * b + RING2 * u + s
                    sp.wait_ge(normalised, 2 * n + 2)
                    if more:
                        read(n + RING2, s)
                    write(b, RING2 * u + s, s)

            with sp.Fori(0, B - 1) as b:
                with sp.Fori(0, TILES // RING2) as u:
                    ring(b, u, True)
            with sp.Fori(0, TILES // RING2 - 1) as u:
                ring(B - 1, u, True)
            ring(B - 1, TILES // RING2 - 1, False)
            for s in range(RING2):
                sp.wait_ge(out_written[s], 16 * B * TILES // RING2)

        @block.gpsimd
        def _(pool):
            nc.gpsimd.memset(zeros[:, :], 0.0).then_inc(zeros_set, 1)
            nc.gpsimd.memset(x_tile[2 * CI:P, :, LOADED - 1, :], 0.0).then_inc(zeros_set, 1)
            pool.wait_ge(zeros_set, 2)
            nc.gpsimd.memset(ident[:, :], 0.0).then_inc(sel_cleared, 1)
            nc.gpsimd.memset(same_channel[:, :, :], 0.0).then_inc(sel_cleared, 1)
            nc.gpsimd.memset(ones[:, :], 1.0).then_inc(consts_set, 1)
            pool.wait_ge(sel_cleared, 2)
            nc.gpsimd.affine_select(out=ident[:, :], in_=ident[:, :], compare_op=ALU.not_equal, fill=1.0,
                                    base=0, pattern=[[-1, P]], channel_multiplier=1).then_inc(consts_set, 1)
            for off in range(G):
                pool.wait_ge(sel_cleared, 2 + off)
                nc.gpsimd.affine_select(out=same_channel[:, :, :], in_=same_channel[:, :, :],
                                        compare_op=ALU.not_equal, fill=1.0 / G, base=-off,
                                        pattern=[[-G, CO], [0, G]],
                                        channel_multiplier=1).then_inc(sel_cleared, 1)

        def split_view(t, slot):
            return t[:, slot, 0:WIN + 1:2, :].rearrange("p w (f c) -> p w f c", f=2)[:, :, :, 0:X]

        def x_view(slot):
            return x_tile[:, slot, :, :].rearrange("p w (c f) -> p w f c", f=2)

        def upper_of_odd(t, slot):
            return t[2 * CI:P, slot, 1:WIN:2, :], t[0:2 * CI, slot, 2:WIN + 1:2, :].bitcast(F32)

        def lower_of_odd(t, slot):
            return t[0:2 * CI, slot, 1:WIN:2, :], t[2 * CI:P, slot, 0:WIN:2, :].bitcast(F32)

        @block.scalar
        def _(act):
            def sum_channel(c, slot):
                nc.scalar.activation(arena[:, slot, :], arena[:, slot, :], ACT.Copy,
                                     accum_out=sums[:, bass.ds(c, 1)]).then_inc(pool_summed, 1)

            def sum_next(b, c, s):
                act.wait_ge(pool_loaded[s], 8 * (CI * (b - 1) + c - s) + 16)
                sum_channel(c, 2 + s)

            def exponentials(b):
                act.wait_ge(logits_ready, b + 1)
                nc.scalar.activation(expo[:, :], logit[:, :], ACT.Exp, bias=small[:, 0:1],
                                     accum_out=small[:, 1:2]).then_inc(exp_ready, 1)

            def split_head(b, t, slot):
                act.wait_ge(x_loaded[slot], 40 * (TILES * b + t - slot) + 80)
                nc.scalar.activation(split_view(head, slot), x_view(slot), ACT.Copy).then_inc(head_ready, 1)

            def copy_head(n, slot):
                act.wait_ge(head_ready, n + 1)
                to, of = lower_of_odd(head, slot)
                nc.scalar.activation(to, of, ACT.Copy).then_inc(odd_head_low_ready, 1)

            def copy_pair(n, half, slot):
                act.wait_ge(pair_done, PAIRS * n + half + 1)
                bank = 4 * slot + 2 * half
                nc.scalar.activation(raw_tile[:, slot, 4 * half:4 * half + 4, :].rearrange("p w c -> p (w c)"),
                                     ps[:, bank:bank + 2, :].rearrange("p a n -> p (a n)"),
                                     ACT.Copy).then_inc(raw_copied, 1)

            def write_raw(n, slot):
                act.wait_ge(raw_copied, PAIRS * n + PAIRS)
                dst = raw[bass.ds(n, 1), :, :, :, :].rearrange("n o q w x -> (n o q) w x")
                act.dma_start(dst, raw_tile[:, slot, :, :]).then_inc(raw_written[slot], 16)

            with act.Fori(0, CI // 4) as u:
                for s in range(4):
                    act.wait_ge(first_loaded[s], 16 * u + 16)
                    sum_channel(4 * u + s, s)
            exponentials(0)
            act.wait_ge(zeros_set, 2)
            split_head(0, 0, 0)
            copy_head(0, 0)

            def step(b, t, slot):
                n = TILES * b + t
                other = 1 - slot
                if not fixed(n) or n >= 1:
                    copy_pair(n - 1, 1, other)
                    write_raw(n - 1, other)
                last = fixed(n) and n == B * TILES - 1
                if not last:
                    if fixed(t) and t == TILES - 1:
                        split_head(b + 1, 0, other)
                    else:
                        split_head(b, t + 1, other)
                    copy_head(n + 1, other)
                pool_next(b, t, other)
                if not fixed(n) or n >= 2:
                    act.wait_ge(raw_written[slot], 8 * (n - slot))
                    act.wait_ge(stats_done, PAIRS * n - 2)
                copy_pair(n, 0, slot)

            def pool_next(b, t, other):
                if not (fixed(b) and b == B - 1):
                    if fixed(t) and t == 0:
                        act.wait_ge(pool_total, b + 1)
                        sum_next(b + 1, 0, 0)
                        sum_next(b + 1, 1, 1)
                    elif fixed(t) and t == TILES - 1:
                        exponentials(b + 1)
                    else:
                        sum_next(b + 1, t + 1, other)

            all_samples(act, lambda b: tiles_of_sample(act, b, step))
            copy_pair(B * TILES - 1, 1, 1)
            write_raw(B * TILES - 1, 1)

            act.wait_ge(varsum_ready, 1)
            nc.scalar.activation(fin[:, 3:4], fin[:, 2:3], ACT.Sqrt).then_inc(sqrt_ready, 1)
            act.wait_ge(scale_ready, 1)
            def normalise(u):
                for s in range(RING2):
                    act.wait_ge(read_loaded[s], 64 * u + 64)
                    if not fixed(u):
                        act.wait_ge(out_written[s], 16 * u)
                    elif s < 2:
                        act.wait_ge(raw_written[s], 16 * B * TILES // 2)
                    for f in range(2):
                        nc.scalar.activation(norm_tile[:, s, f, :, :, :], read_tile[:, s, :, f, :, :], ACT.Relu,
                                             bias=shift[:, 0:1], scale=scale[:, 0:1]).then_inc(normalised, 1)

            normalise(0)
            with act.Fori(1, B * TILES // RING2) as u:
                normalise(u)

        @block.vector
        def _(dve):
            for t in (head, rest):
                pads = t[:, :, :, :].rearrange("p s w (f c) -> p (s w) f c", f=2)[:, :, :, X:]
                nc.vector.memset(pads.bitcast(F32), 0.0).then_inc(k_rows_set, 1)
            nc.vector.memset(w_each[:, :, :, :, :, :], 0.0).then_inc(k_rows_set, 1)
            nc.vector.memset(k_rows[:, :, :, :, :], 0.0).then_inc(k_rows_set, 1)
            nc.vector.memset(triples[:, :, :], float(H * W // G)).then_inc(k_rows_set, 1)
            dve.wait_ge(kernels_loaded, 16)
            dve.wait_ge(k_rows_set, 4)
            for ro in range(2):
                nc.vector.tensor_copy(k_rows[:, ro, :, ro:ro + KS, :],
                                      k_raw[:, :, :, :].rearrange("p i u v -> p v u i")).then_inc(k_rows_set, 1)
            dve.wait_ge(taps_turned, 1)
            for ro in range(2):
                for dx in range(KS):
                    i = ro * KS + dx
                    turned = ps[:, i // 4, (i % 4) * P:(i % 4 + 1) * P].rearrange("p (k o) -> p k o", k=K)
                    for f in range(2):
                        last = nc.vector.tensor_copy(w_each[:, :, dx + f, :, ro, f], turned)
            last.then_inc(w_each_done, 1)

            def attention(b):
                k0 = ATT_STEPS * b
                dve.wait_ge(pool_total, b + 1)
                nc.vector.tensor_scalar(pooled[:, :], ps[:, 7, 0:CI], 1.0 / (H * W), None,
                                        ALU.mult).then_inc(pool_total_read, 1)
                dve.wait_ge(pool_total_read, b + 1)
                nc.vector.tensor_tensor(prod[:, :, :], watt[:, :, :],
                                        pooled[:, :].unsqueeze(1).to_broadcast([P, K, CI]),
                                        ALU.mult).then_inc(att_chain, 1)
                dve.wait_ge(att_chain, k0 + 1)
                nc.vector.tensor_reduce(logit[:, :], prod[:, :, :], AX_X, ALU.add).then_inc(att_chain, 1)
                dve.wait_ge(att_chain, k0 + 2)
                nc.vector.tensor_tensor(logit[:, :], logit[:, :], batt[:, :], ALU.add).then_inc(att_chain, 1)
                dve.wait_ge(att_chain, k0 + 3)
                nc.vector.tensor_reduce(small[:, 2:3], logit[:, :], AX_X, ALU.max).then_inc(att_chain, 1)
                dve.wait_ge(att_chain, k0 + 4)
                nc.vector.tensor_scalar(small[:, 0:1], small[:, 2:3], -1.0, None, ALU.mult).then_inc(logits_ready, 1)

            def combine(b):
                k0 = ATT_STEPS * b
                dve.wait_ge(exp_ready, b + 1)
                nc.vector.reciprocal(small[:, 3:4], small[:, 1:2]).then_inc(att_chain, 1)
                dve.wait_ge(att_chain, k0 + 5)
                nc.vector.tensor_scalar(att[:, :], expo[:, :], small[:, 3:4], None, ALU.mult).then_inc(att_chain, 1)
                dve.wait_ge(att_chain, k0 + 6)
                for k in range(K):
                    one = w_each[:, k, :, :, :, :].rearrange("p s o r f -> p (s o r f)")
                    if k == 0:
                        last = nc.vector.tensor_scalar(w_sum[:, :], one, att[:, 0:1], None, ALU.mult)
                    else:
                        last = nc.vector.scalar_tensor_tensor(out=w_sum[:, :], in0=one, scalar=att[:, k:k + 1],
                                                              in1=w_sum[:, :], op0=ALU.mult, op1=ALU.add)
                    last.then_inc(att_chain, 1)
                    dve.wait_ge(att_chain, k0 + 7 + k)

            def split_weights(b):
                flat = w_head[:, :, :].rearrange("p s m -> p (s m)")
                if not fixed(b) or b > 0:
                    dve.wait_ge(pair_done, PAIRS * TILES * b)
                nc.vector.tensor_copy(flat, w_sum[:, :]).then_inc(weights_ready, 1)
                dve.wait_ge(weights_ready, 2 * b + 1)
                nc.vector.tensor_tensor(w_rest[:, :, :].rearrange("p s m -> p (s m)"), w_sum[:, :],
                                        flat.bitcast(F32), ALU.subtract).then_inc(weights_ready, 1)

            def split_rest(n, slot):
                dve.wait_ge(head_ready, n + 1)
                nc.vector.tensor_tensor(split_view(rest, slot), x_view(slot), split_view(head, slot).bitcast(F32),
                                        ALU.subtract).then_inc(rest_ready, 1)

            def copy_odd(n, slot):
                to, of = upper_of_odd(head, slot)
                nc.vector.tensor_copy(to, of).then_inc(odd_head_up_ready, 1)
                dve.wait_ge(rest_ready, n + 1)
                for half in (lower_of_odd, upper_of_odd):
                    to, of = half(rest, slot)
                    nc.vector.tensor_copy(to, of).then_inc(odd_rest_ready, 1)

            def pair_stats(n, t, half, slot):
                dve.wait_ge(raw_copied, PAIRS * n + half + 1)
                for a in range(2):
                    last = nc.vector.bn_stats(stats[:, bass.ds(4 * t + 2 * half + a, 1), :].rearrange("p o s -> p (o s)"),
                                              raw_tile[:, slot, 4 * half + 2 * a:4 * half + 2 * a + 2, :]
                                              .rearrange("p w c -> p (w c)"))
                last.then_inc(stats_done, 1)

            def tile_stats(n, t, slot):
                for half in range(PAIRS):
                    pair_stats(n, t, half, slot)

            def aggregate(b):
                dve.wait_ge(stats_done, PAIRS * TILES * (b + 1))
                nc.vector.memset(count[:, :], float(H * W // G))
                nc.vector.bn_aggr(sample_mv[:, :], stats[:, :, :].rearrange("p c s -> p (c s)")).then_inc(aggr_done, 1)
                dve.wait_ge(aggr_done, 3 * b + 1)
                one = triples[:, bass.ds(b, 1), :].rearrange("p o s -> p (o s)")
                nc.vector.tensor_copy(one[:, 1:2], sample_mv[:, 0:1]).then_inc(aggr_done, 1)
                nc.vector.tensor_scalar(one[:, 2:3], sample_mv[:, 1:2], float(H * W // G), None,
                                        ALU.mult).then_inc(aggr_done, 1)
                dve.wait_ge(aggr_done, 3 * b + 3)

            dve.wait_ge(params_loaded, 16 * 10)
            attention(0)
            combine(0)
            split_weights(0)
            split_rest(0, 0)
            copy_odd(0, 0)

            def step(b, t, slot):
                n = TILES * b + t
                other = 1 - slot
                last_sample = fixed(b) and b == B - 1
                final = fixed(t) and t == TILES - 1
                if final and not last_sample:
                    attention(b + 1)
                if fixed(t) and t == 0:
                    if not fixed(b) or b > 0:
                        tile_stats(n - 1, TILES - 1, other)
                        aggregate(b - 1)
                else:
                    tile_stats(n - 1, t - 1, other)
                if not (final and last_sample):
                    split_rest(n + 1, other)
                    copy_odd(n + 1, other)
                if final and not last_sample:
                    combine(b + 1)
                    split_weights(b + 1)

            all_samples(dve, lambda b: tiles_of_sample(dve, b, step))
            tile_stats(B * TILES - 1, TILES - 1, 1)
            aggregate(B - 1)

            chain = [0]

            def link(ins):
                chain[0] += 1
                ins.then_inc(fin_chain, 1)
                dve.wait_ge(fin_chain, chain[0])

            nc.vector.bn_aggr(total[:, :], triples[:, :, :].rearrange("p b s -> p (b s)")).then_inc(mean_ready, 1)
            dve.wait_ge(meansum_ready, 1)
            link(nc.vector.tensor_copy(fin[:, 0:1], ps[:, 0, 0:1]))
            link(nc.vector.tensor_tensor(fin[:, 4:5], total[:, 0:1], fin[:, 0:1], ALU.subtract))
            link(nc.vector.tensor_tensor(fin[:, 5:6], fin[:, 4:5], fin[:, 4:5], ALU.mult))
            nc.vector.tensor_tensor(fin[:, 1:2], fin[:, 5:6], total[:, 1:2], ALU.add).then_inc(dev_ready, 1)
            dve.wait_ge(var_ready, 1)
            nc.vector.tensor_scalar(fin[:, 2:3], ps[:, 1, 0:1], EPS, None, ALU.add).then_inc(varsum_ready, 1)
            dve.wait_ge(sqrt_ready, 1)
            link(nc.vector.reciprocal(fin[:, 6:7], fin[:, 3:4]))
            link(nc.vector.tensor_tensor(fin[:, 7:8], fin[:, 6:7], fin[:, 6:7], ALU.mult))
            link(nc.vector.tensor_tensor(fin[:, 8:9], fin[:, 7:8], fin[:, 2:3], ALU.mult))
            link(nc.vector.tensor_scalar(fin[:, 9:10], fin[:, 8:9], -0.5, 1.5, ALU.mult, ALU.add))
            link(nc.vector.tensor_tensor(fin[:, 10:11], fin[:, 9:10], fin[:, 6:7], ALU.mult))
            link(nc.vector.tensor_tensor(scale[:, :], fin[:, 10:11], gam[:, :], ALU.mult))
            link(nc.vector.tensor_tensor(fin[:, 11:12], scale[:, :], fin[:, 0:1], ALU.mult))
            nc.vector.tensor_tensor(shift[:, :], bet[:, :], fin[:, 11:12], ALU.subtract).then_inc(scale_ready, 1)

        @block.tensor
        def _(pe):
            pe.wait_ge(k_rows_set, 7)
            pe.wait_ge(consts_set, 2)
            for ro in range(2):
                for dx in range(KS):
                    i = ro * KS + dx
                    rows = k_rows[:, ro, dx, :, :].rearrange("p g i -> p (g i)")
                    last = nc.tensor.matmul(ps[:, i // 4, (i % 4) * P:(i % 4 + 1) * P], rows, ident[:, :],
                                            start=True, stop=True)
            last.then_inc(taps_turned, 1)

            def total_pool(b):
                pe.wait_ge(pool_summed, CI * (b + 1))
                nc.tensor.matmul(ps[:, 7, 0:CI], ones[:, :], sums[:, :], start=True, stop=True).then_inc(pool_total, 1)

            total_pool(0)

            def step(b, t, slot):
                n = TILES * b + t
                if not fixed(n) or n >= 2:
                    pe.wait_ge(raw_copied, PAIRS * n - 2)
                if fixed(t) and t == 0:
                    pe.wait_ge(weights_ready, 2 * b + 2)
                last_tile = fixed(t) and t == TILES - 1
                if last_tile and not (fixed(b) and b == B - 1):
                    total_pool(b + 1)
                if fixed(n) and n == 1:
                    pe.wait_ge(pool_total_read, 1)
                pe.wait_ge(odd_head_low_ready, n + 1)
                pe.wait_ge(odd_head_up_ready, n + 1)
                for bank in range(4):
                    if bank == 3 and last_tile and not (fixed(b) and b == B - 1):
                        pe.wait_ge(pool_total_read, b + 2)
                    for i, (w, part) in enumerate(((w_head, head), (w_rest, head), (w_head, rest))):
                        if i == 2 and bank == 0:
                            pe.wait_ge(odd_rest_ready, 2 * n + 2)
                        for s in range(TAPS):
                            at = (ODD - 1, 0, ODD, 1)[s]
                            last = nc.tensor.matmul(ps[:, 4 * slot + bank, :], w[:, s, :],
                                                    part[:, slot, 2 * bank:2 * bank + 2, at:at + X],
                                                    start=(i == 0 and s == 0), stop=(i == 2 and s == TAPS - 1))
                    if bank % 2:
                        last.then_inc(pair_done, 1)

            all_samples(pe, lambda b: tiles_of_sample(pe, b, step))

            pe.wait_ge(sel_cleared, 6)
            pe.wait_ge(mean_ready, 1)
            pe.wait_ge(raw_copied, PAIRS * B * TILES)
            sel = same_channel[:, :, :].rearrange("p c g -> p (c g)")
            nc.tensor.matmul(ps[:, 0, 0:1], sel, total[:, 0:1], start=True, stop=True).then_inc(meansum_ready, 1)
            pe.wait_ge(dev_ready, 1)
            nc.tensor.matmul(ps[:, 1, 0:1], sel, fin[:, 1:2], start=True, stop=True).then_inc(var_ready, 1)


_INS = ['x', 'L0_conv_kernels', 'L0_conv_w_att', 'L0_conv_b_att', 'L0_conv_gamma', 'L0_conv_beta']


def kernel(**inputs):
    import numpy as _np
    import concourse.bacc as _bacc
    from concourse import mybir as _mybir
    from concourse.bass_utils import run_bass_kernel_spmd as _run

    nc = _bacc.Bacc("TRN2", target_bir_lowering=False, num_devices=1)
    arrays, args = {}, []
    for name in _INS:
        a = _np.ascontiguousarray(inputs[name])
        arrays[f"in_{name}_dram"] = a
        args.append(nc.dram_tensor(f"in_{name}_dram", a.shape, _mybir.dt.from_np(a.dtype), kind="ExternalInput").ap())
    shape = inputs['x'].shape[:1] + (inputs['L0_conv_kernels'].shape[1],) + inputs['x'].shape[2:]
    args.append(nc.dram_tensor("out_dram", shape, _mybir.dt.float32, kind="ExternalOutput").ap())
    dynamic_conv_batchnorm_relu(nc, *args)
    r = _run(nc, [arrays], core_ids=[0])
    return r.results[0]["out_dram"]
```

```python
from contextlib import ExitStack

import concourse.bass as bass
from concourse import mybir

ALU = mybir.AluOpType
ACT = mybir.ActivationFunctionType
AX_X = mybir.AxisListType.X
F32 = mybir.dt.float32
F32R = mybir.dt.float32r

P = 128
EPS = 1e-5


def dynamic_conv_batchnorm_relu(
    nc: bass.Bass,
    x: bass.AP,
    kernels: bass.AP,
    w_att: bass.AP,
    b_att: bass.AP,
    gamma: bass.AP,
    beta: bass.AP,
    out: bass.AP,
):
    B, CI, H, W = x.shape
    K, CO, _, KS, _ = kernels.shape
    assert (CI, CO, KS) == (32, 32, 3) and K * CO == P
    TAPS = KS + 1
    X = W // 2
    WIN = 8
    TILES = H // (2 * WIN)
    LOADED = WIN // 2 + 1
    PAIRS = 2
    G = P // CI
    ROW = 2 * (X + 3)
    ODD = X + 3
    FLAT = H * W // P
    BANK = 512
    CHUNKS = TILES * 4
    RING_OUT = 4
    RING_IN = 8

    assert TILES % 2 == 0 and CI == TILES

    with ExitStack() as ctx:
        def sb(name, shape, dt=F32):
            return ctx.enter_context(nc.sbuf_tensor(name, shape, dt))

        def sem(name):
            return ctx.enter_context(nc.semaphore(name))

        TILE_ELEMENTS = CO * 2 * WIN * W
        PITCH = TILE_ELEMENTS + 1024
        raws = [nc.dram_tensor(f"raw_conv{i}", [B // 2 * TILES, PITCH], F32, kind="Internal").ap() for i in range(2)]

        arena = sb("arena", [P, 4, FLAT])
        raw_tile = arena[:, 0:2, :].rearrange("p s (w c) -> p s w c", w=WIN)
        norm_tile = arena[:, :, :].rearrange("p s (j r c f) -> p s f r j c", j=2, r=2, f=2)
        x_tile = sb("x_tile", [P, 2, LOADED, W])
        ahead = sb("ahead", [P, RING_IN - 1, FLAT])
        read_tile = [ahead[:, i, :] for i in range(RING_IN - 1)]
        read_tile += [x_tile[:, 0, :, :].rearrange("p v x -> p (v x)")[:, 0:FLAT]]

        head = sb("head", [P, 2, WIN + 1, ROW], F32R)
        rest = sb("rest", [P, 2, WIN + 1, ROW], F32R)
        w_head = sb("w_head", [P, TAPS, P], F32R)
        w_rest = sb("w_rest", [P, TAPS, P], F32R)
        w_sum = sb("w_sum", [P, TAPS * P])
        w_each = sb("w_each", [P, K, TAPS, CO, 2, 2])
        k_raw = ahead[:, 0, 0:CI * KS * KS].rearrange("p (i u v) -> p i u v", i=CI, u=KS)
        k_rows = ahead[:, 1, 0:2 * KS * P].rearrange("p (r v g i) -> p r v g i", r=2, v=KS, g=G)
        ident = ahead[:, 2, 0:P]
        ones = sb("ones", [P, P])
        same_channel = sb("same_channel", [P, CO, G])
        zeros = sb("zeros", [CI, W])
        sums = sb("sums", [P, CI])
        pooled = sb("pooled", [P, CI])
        watt = sb("watt", [P, K, CI])
        batt = sb("batt", [P, K])
        prod = sb("prod", [P, K, CI])
        logit = sb("logit", [P, K])
        small = sb("small", [P, 4])
        expo = sb("expo", [P, K])
        att = sb("att", [P, K])
        stats = sb("stats", [P, CHUNKS, 6])
        triples = sb("triples", [P, B, 3])
        count = sb("count", [P, 1])
        sample_mv = sb("sample_mv", [P, 2])
        total = sb("total", [P, 2])
        own = sb("own", [P, 4])
        by_channel = sb("by_channel", [P, 8, CO])
        gam = sb("gam", [P, CO])
        bet = sb("bet", [P, CO])
        scale = sb("scale", [P, CO])
        shift = sb("shift", [P, CO])
        ps = ctx.enter_context(nc.psum_tensor("ps", [P, 8, BANK], F32))

        params_loaded = sem("params_loaded")
        kernels_loaded = sem("kernels_loaded")
        first_loaded = [sem(f"first_loaded{i}") for i in range(4)]
        x_loaded = [sem(f"x_loaded{i}") for i in range(2)]
        pool_loaded = [sem(f"pool_loaded{i}") for i in range(2)]
        raw_written = [sem(f"raw_written{i}") for i in range(2)]
        read_loaded = [sem(f"read_loaded{i}") for i in range(RING_IN)]
        out_written = [sem(f"out_written{i}") for i in range(RING_OUT)]
        pool_summed = sem("pool_summed")
        zeros_set = sem("zeros_set")
        consts_set = sem("consts_set")
        same_channel_set = sem("same_channel_set")
        buffers_set = sem("buffers_set")
        k_rows_set = sem("k_rows_set")
        taps_turned = sem("taps_turned")
        w_each_done = sem("w_each_done")
        pool_total = sem("pool_total")
        pool_total_read = sem("pool_total_read")
        logits_ready = sem("logits_ready")
        exp_ready = sem("exp_ready")
        w_sum_chain = sem("w_sum_chain")
        w_head_ready = sem("w_head_ready")
        w_rest_ready = sem("w_rest_ready")
        w_head_used = sem("w_head_used")
        att_chain = sem("att_chain")
        head_ready = sem("head_ready")
        rest_ready = sem("rest_ready")
        odd_head_low_ready = sem("odd_head_low_ready")
        odd_head_up_ready = sem("odd_head_up_ready")
        odd_rest_ready = sem("odd_rest_ready")
        pair_done = sem("pair_done")
        raw_copied = sem("raw_copied")
        stats_done = sem("stats_done")
        aggr_done = sem("aggr_done")
        fin_chain = sem("fin_chain")
        mean_ready = sem("mean_ready")
        var_ready = sem("var_ready")
        dev_ready = sem("dev_ready")
        meansum_ready = sem("meansum_ready")
        varsum_ready = sem("varsum_ready")
        sqrt_ready = sem("sqrt_ready")
        scale_ready = sem("scale_ready")
        normalised = sem("normalised")

        ATT_STEPS = 4
        W_SUM_STEPS = 2 + K

        def tiles_of_sample(eng, b, step):
            step(b, 0, 0)
            step(b, 1, 1)
            with eng.Fori(1, TILES // 2 - 1) as j:
                step(b, 2 * j, 0)
                step(b, 2 * j + 1, 1)
            step(b, TILES - 2, 0)
            step(b, TILES - 1, 1)

        def all_samples(eng, sample):
            sample(0, 0)
            with eng.Fori(1, B // 2) as b:
                sample(b, 0)
            with eng.Fori(B // 2, B - 1) as b:
                sample(b, 1)
            sample(B - 1, 1)

        def fixed(v):
            return isinstance(v, int)

        def pooled_beside(t, slot):
            if fixed(t) and t < 2:
                return [(2 * t, 0), (2 * t + 1, 1)]
            if fixed(t) and t >= TILES - 2:
                return []
            return [(t + 2, slot)]

        block = ctx.enter_context(nc.Block())

        @block.sync
        def _(sp):
            sp.dma_start(k_raw[:, :, :, :], kernels.rearrange("k o i u v -> (k o) i u v")).then_inc(kernels_loaded, 16)

            def load_channel(b, c, slot, signal):
                src = x[bass.ds(b, 1), bass.ds(c, 1), :, :].rearrange("b c (p h) w -> (b c p) (h w)", p=P)
                sp.dma_start(arena[:, slot, :], src).then_inc(signal, 16)

            for c in range(4):
                load_channel(0, c, c, first_loaded[c])
            sp.dma_start(watt[:, :, :], w_att.partition_broadcast(P)).then_inc(params_loaded, 16)
            sp.dma_start(batt[:, :], b_att.partition_broadcast(P)).then_inc(params_loaded, 16)
            sp.dma_start(gam[:, :], gamma.partition_broadcast(P)).then_inc(params_loaded, 16)
            sp.dma_start(bet[:, :], beta.partition_broadcast(P)).then_inc(params_loaded, 16)

            def load_x(b, t, slot):
                top, bottom = fixed(t) and t == 0, fixed(t) and t == TILES - 1
                for g in range(G):
                    cuts = [(0, LOADED if g < 2 else LOADED - 1)]
                    if bottom and g == 1:
                        cuts = [(0, LOADED - 1), (LOADED - 1, LOADED)]
                    if not bottom and g == 0:
                        cuts = [(0, 1), (1, LOADED)]
                    for v0, v1 in cuts:
                        dst = x_tile[g * CI:(g + 1) * CI, slot, v0:v1, :]
                        if (top and g == 0 and v0 == 0) or (bottom and g == 1 and v0 == LOADED - 1):
                            src = zeros[:, :].unsqueeze(1)
                        else:
                            at = 2 * WIN * t + 4 * v0 - (4 if g == 0 else 0)
                            src = x[bass.ds(b, 1), :, bass.ds(at, 4 * (v1 - v0)), :]
                            src = src.rearrange("b c (v o) x -> (b c) v o x", o=4)[:, :, (g - 1) % 4, :]
                        sp.dma_start(dst, src).then_inc(x_loaded[slot], 16)

            with sp.Fori(1, CI // 4) as u:
                for s in range(4):
                    sp.wait_ge(pool_summed, 4 * u + s - 3)
                    load_channel(0, 4 * u + s, s, first_loaded[s])

            def tile(b, t, slot, channels):
                n = TILES * b + t
                if fixed(n) and n == 0:
                    sp.wait_ge(zeros_set, 2)
                if not fixed(n) or n >= 2:
                    sp.wait_ge(rest_ready, n - 1)
                load_x(b, t, slot)
                if fixed(b) and b == B - 1:
                    return
                for c, s in channels:
                    sp.wait_ge(pool_summed, CI * (b + 1) + c - 1)
                    load_channel(b + 1, c, 2 + s, pool_loaded[s])

            def sample(b, i):
                tile(b, 0, 0, [])
                tile(b, 1, 1, [(0, 0), (1, 1)])
                tile(b, 2, 0, [(2, 0), (3, 1)])
                with sp.Fori(1, TILES // 2 - 2) as j:
                    tile(b, 2 * j + 1, 1, [(2 * j + 2, 0)])
                    tile(b, 2 * j + 2, 0, [(2 * j + 3, 1)])
                tile(b, TILES - 3, 1, [(CI - 2, 0)])
                tile(b, TILES - 2, 0, [(CI - 1, 1)])
                tile(b, TILES - 1, 1, [])

            all_samples(sp, sample)

            def read(b, c, slot, i):
                tiles = raws[i][bass.ds(TILES * (b - i * B // 2), TILES), 0:TILE_ELEMENTS]
                tiles = tiles.rearrange("t (o q w x) -> t o q w x", o=CO, q=G, w=WIN)
                for jb in range(G):
                    src = tiles[:, bass.ds(c, 1), :, 2 * jb:2 * jb + 2, :].rearrange("t o q j x -> (t o) q (j x)")
                    dst = read_tile[slot][jb:P:G, :].rearrange("p (q x) -> p q x", q=G)
                    sp.dma_start(dst, src).then_inc(read_loaded[slot], 16)

            def write(b, c, slot):
                dst = out[bass.ds(b, 1), bass.ds(c, 1), :, :].rearrange("b c (p r) x -> (b c p) (r x)", p=P)
                slot = slot % RING_OUT
                sp.dma_start(dst, arena[:, slot, :]).then_inc(out_written[slot], 16)

            for s in range(2):
                sp.wait_ge(raw_written[s], 16 * TILES // 2)
            for s in range(RING_IN):
                if s == RING_IN - 1:
                    sp.wait_ge(rest_ready, B * TILES)
                read(0, s, s, 0)
            for s in range(2):
                sp.wait_ge(raw_written[s], 16 * B * TILES // 2)

            def ring(b, u, next_b, next_u, i):
                for s in range(RING_IN):
                    sp.wait_ge(normalised, 2 * (CO * b + RING_IN * u + s) + 2)
                    if next_b is not None:
                        read(next_b, RING_IN * next_u + s, s, i)
                    write(b, RING_IN * u + s, s)

            def channels(b, i):
                with sp.Fori(0, CO // RING_IN - 1) as u:
                    ring(b, u, b, u + 1, i)

            LAST_U = CO // RING_IN - 1
            for i in range(2):
                with sp.Fori(i * B // 2, (i + 1) * B // 2 - 1) as b:
                    channels(b, i)
                    ring(b, LAST_U, b + 1, 0, i)
                b = (i + 1) * B // 2 - 1
                channels(b, i)
                if i == 0:
                    ring(b, LAST_U, b + 1, 0, 1)
                else:
                    ring(b, LAST_U, None, None, 1)
            for s in range(RING_OUT):
                sp.wait_ge(out_written[s], 16 * B * CO // RING_OUT)

        @block.gpsimd
        def _(pool):
            nc.gpsimd.memset(zeros[:, :], 0.0).then_inc(zeros_set, 1)
            nc.gpsimd.memset(x_tile[2 * CI:P, :, LOADED - 1, :], 0.0).then_inc(zeros_set, 1)
            pool.wait_ge(zeros_set, 2)
            nc.gpsimd.memset(ones[:, :], 1.0).then_inc(consts_set, 1)
            nc.gpsimd.memset(ident[:, :], 0.0).then_inc(consts_set, 1)
            nc.gpsimd.memset(same_channel[:, :, :], 0.0).then_inc(same_channel_set, 1)
            pool.wait_ge(consts_set, 2)
            nc.gpsimd.affine_select(out=ident[:, :], in_=ident[:, :], compare_op=ALU.not_equal, fill=1.0,
                                    base=0, pattern=[[-1, P]], channel_multiplier=1).then_inc(consts_set, 1)
            for off in range(G):
                pool.wait_ge(same_channel_set, 1 + off)
                nc.gpsimd.affine_select(out=same_channel[:, :, :], in_=same_channel[:, :, :],
                                        compare_op=ALU.not_equal, fill=1.0 / G, base=-off,
                                        pattern=[[-G, CO], [0, G]],
                                        channel_multiplier=1).then_inc(same_channel_set, 1)

        def split_view(t, slot):
            return t[:, slot, 0:WIN + 1:2, :].rearrange("p w (f c) -> p w f c", f=2)[:, :, :, 0:X]

        def x_view(slot):
            return x_tile[:, slot, :, :].rearrange("p w (c f) -> p w f c", f=2)

        def upper_of_odd(t, slot):
            return t[2 * CI:P, slot, 1:WIN:2, :], t[0:2 * CI, slot, 2:WIN + 1:2, :].bitcast(F32)

        def lower_of_odd(t, slot):
            return t[0:2 * CI, slot, 1:WIN:2, :], t[2 * CI:P, slot, 0:WIN:2, :].bitcast(F32)

        @block.scalar
        def _(act):
            def sum_channel(c, slot):
                nc.scalar.activation(arena[:, slot, :], arena[:, slot, :], ACT.Copy,
                                     accum_out=sums[:, bass.ds(c, 1)]).then_inc(pool_summed, 1)

            def sum_next(b, c, s):
                act.wait_ge(pool_loaded[s], 8 * (CI * (b - 1) + c - s) + 16)
                sum_channel(c, 2 + s)

            def exponentials(b):
                act.wait_ge(logits_ready, b + 1)
                nc.scalar.activation(expo[:, :], logit[:, :], ACT.Exp, bias=small[:, 0:1],
                                     accum_out=small[:, 1:2]).then_inc(exp_ready, 1)

            def split_head(b, t, slot):
                act.wait_ge(x_loaded[slot], 40 * (TILES * b + t - slot) + 80)
                nc.scalar.activation(split_view(head, slot), x_view(slot), ACT.Copy).then_inc(head_ready, 1)

            def split_w_head(b):
                act.wait_ge(w_sum_chain, W_SUM_STEPS * (b + 1))
                if not fixed(b) or b > 0:
                    act.wait_ge(w_head_used, b)
                nc.scalar.activation(w_head[:, :, :].rearrange("p s m -> p (s m)"), w_sum[:, :],
                                     ACT.Copy).then_inc(w_head_ready, 1)

            def copy_head(n, slot):
                act.wait_ge(head_ready, n + 1)
                to, of = lower_of_odd(head, slot)
                nc.scalar.activation(to, of, ACT.Copy).then_inc(odd_head_low_ready, 1)

            def copy_pair(n, half, slot):
                act.wait_ge(pair_done, PAIRS * n + half + 1)
                bank = 4 * slot + 2 * half
                nc.scalar.activation(raw_tile[:, slot, 4 * half:4 * half + 4, :].rearrange("p w c -> p (w c)"),
                                     ps[:, bank:bank + 2, :].rearrange("p a n -> p (a n)"),
                                     ACT.Copy).then_inc(raw_copied, 1)

            def write_raw(n, slot, i):
                act.wait_ge(raw_copied, PAIRS * n + PAIRS)
                dst = raws[i][bass.ds(n - i * B // 2 * TILES, 1), 0:TILE_ELEMENTS].rearrange("n (p x) -> (n p) x", p=P)
                act.dma_start(dst, raw_tile[:, slot, :, :].rearrange("p w x -> p (w x)")).then_inc(raw_written[slot], 16)

            with act.Fori(0, CI // 4) as u:
                for s in range(4):
                    act.wait_ge(first_loaded[s], 16 * u + 16)
                    sum_channel(4 * u + s, s)
            exponentials(0)
            act.wait_ge(zeros_set, 2)
            split_head(0, 0, 0)
            split_w_head(0)
            copy_head(0, 0)

            def step(b, t, slot, i):
                n = TILES * b + t
                other = 1 - slot
                if not (fixed(t) and t == 0):
                    copy_pair(n - 1, 1, other)
                    write_raw(n - 1, other, i)
                last = fixed(n) and n == B * TILES - 1
                if not last:
                    if fixed(t) and t == TILES - 1:
                        split_head(b + 1, 0, other)
                    else:
                        split_head(b, t + 1, other)
                    copy_head(n + 1, other)
                pool_next(b, t, slot)
                if not fixed(n) or n >= 2:
                    act.wait_ge(raw_written[slot], 8 * (n - slot))
                    act.wait_ge(stats_done, PAIRS * n - 2)
                copy_pair(n, 0, slot)
                if fixed(t) and t == TILES - 1:
                    if not (fixed(b) and b == B - 1):
                        split_w_head(b + 1)
                    copy_pair(n, 1, slot)
                    write_raw(n, slot, i)

            def pool_next(b, t, slot):
                if fixed(b) and b == B - 1:
                    return
                if fixed(t) and t == 0:
                    act.wait_ge(pool_total, b + 1)
                for c, s in pooled_beside(t, slot):
                    sum_next(b + 1, c, s)
                if fixed(t) and t == TILES - 2:
                    exponentials(b + 1)

            all_samples(act, lambda b, i: tiles_of_sample(act, b, lambda b, t, slot: step(b, t, slot, i)))

            act.wait_ge(varsum_ready, 1)
            nc.scalar.activation(by_channel[:, 2, :], by_channel[:, 1, :], ACT.Sqrt).then_inc(sqrt_ready, 1)
            act.wait_ge(scale_ready, 1)

            def normalise(b, u, first=False):
                for s in range(RING_IN):
                    act.wait_ge(read_loaded[s], 64 * (CO // RING_IN * b + u) + 64)
                    so = s % RING_OUT
                    if not first or s >= RING_OUT:
                        act.wait_ge(out_written[so], 16 * (CO // RING_OUT * b + RING_IN // RING_OUT * u + s // RING_OUT))
                    elif s < 2:
                        act.wait_ge(raw_written[s], 16 * B * TILES // 2)
                    c = bass.ds(RING_IN * u + s, 1)
                    source = read_tile[s].rearrange("p (r f j x) -> p f r j x", r=2, f=2, j=2)
                    for f in range(2):
                        nc.scalar.activation(norm_tile[:, so, f, :, :, :], source[:, f, :, :, :], ACT.Relu,
                                             bias=shift[:, c], scale=scale[:, c]).then_inc(normalised, 1)

            normalise(0, 0, first=True)
            with act.Fori(1, CO // RING_IN) as u:
                normalise(0, u)
            with act.Fori(1, B) as b:
                with act.Fori(0, CO // RING_IN) as u:
                    normalise(b, u)

        @block.vector
        def _(dve):
            for t in (head, rest):
                pads = t[:, :, :, :].rearrange("p s w (f c) -> p (s w) f c", f=2)[:, :, :, X:]
                nc.vector.memset(pads.bitcast(F32), 0.0).then_inc(buffers_set, 1)
            nc.vector.memset(w_each[:, :, :, :, :, :], 0.0).then_inc(buffers_set, 1)
            nc.vector.memset(k_rows[:, :, :, :, :], 0.0).then_inc(k_rows_set, 1)
            nc.vector.memset(triples[:, :, :], float(H * W // G)).then_inc(buffers_set, 1)
            dve.wait_ge(kernels_loaded, 16)
            dve.wait_ge(k_rows_set, 1)
            for ro in range(2):
                nc.vector.tensor_copy(k_rows[:, ro, :, ro:ro + KS, :],
                                      k_raw[:, :, :, :].rearrange("p i u v -> p v u i")).then_inc(k_rows_set, 1)
            dve.wait_ge(taps_turned, 1)
            dve.wait_ge(buffers_set, 4)
            for ro in range(2):
                for dx in range(KS):
                    i = ro * KS + dx
                    turned = ps[:, i // 4, (i % 4) * P:(i % 4 + 1) * P].rearrange("p (k o) -> p k o", k=K)
                    for f in range(2):
                        last = nc.vector.tensor_copy(w_each[:, :, dx + f, :, ro, f], turned)
            last.then_inc(w_each_done, 1)

            def attention(b):
                k0 = ATT_STEPS * b
                dve.wait_ge(pool_total, b + 1)
                nc.vector.tensor_scalar(pooled[:, :], ps[:, 3, 0:CI], 1.0 / (H * W), None,
                                        ALU.mult).then_inc(pool_total_read, 1)
                dve.wait_ge(pool_total_read, b + 1)
                nc.vector.tensor_tensor(prod[:, :, :], watt[:, :, :],
                                        pooled[:, :].unsqueeze(1).to_broadcast([P, K, CI]),
                                        ALU.mult).then_inc(att_chain, 1)
                dve.wait_ge(att_chain, k0 + 1)
                nc.vector.tensor_reduce(logit[:, :], prod[:, :, :], AX_X, ALU.add).then_inc(att_chain, 1)
                dve.wait_ge(att_chain, k0 + 2)
                nc.vector.tensor_tensor(logit[:, :], logit[:, :], batt[:, :], ALU.add).then_inc(att_chain, 1)
                dve.wait_ge(att_chain, k0 + 3)
                nc.vector.tensor_reduce(small[:, 2:3], logit[:, :], AX_X, ALU.max).then_inc(att_chain, 1)
                dve.wait_ge(att_chain, k0 + 4)
                nc.vector.tensor_scalar(small[:, 0:1], small[:, 2:3], -1.0, None, ALU.mult).then_inc(logits_ready, 1)

            def combine(b):
                k0 = W_SUM_STEPS * b
                dve.wait_ge(exp_ready, b + 1)
                nc.vector.reciprocal(small[:, 3:4], small[:, 1:2]).then_inc(w_sum_chain, 1)
                dve.wait_ge(w_sum_chain, k0 + 1)
                nc.vector.tensor_scalar(att[:, :], expo[:, :], small[:, 3:4], None, ALU.mult).then_inc(w_sum_chain, 1)
                if fixed(b) and b == 0:
                    dve.wait_ge(w_each_done, 1)
                for k in range(K):
                    one = w_each[:, k, :, :, :, :].rearrange("p s o r f -> p (s o r f)")
                    dve.wait_ge(w_sum_chain, k0 + 2 + k)
                    if k == 0:
                        last = nc.vector.tensor_scalar(w_sum[:, :], one, att[:, 0:1], None, ALU.mult)
                    else:
                        last = nc.vector.scalar_tensor_tensor(out=w_sum[:, :], in0=one, scalar=att[:, k:k + 1],
                                                              in1=w_sum[:, :], op0=ALU.mult, op1=ALU.add)
                    last.then_inc(w_sum_chain, 1)

            def split_w_rest(b):
                dve.wait_ge(w_head_ready, b + 1)
                if not fixed(b) or b > 0:
                    dve.wait_ge(pair_done, PAIRS * TILES * b)
                nc.vector.tensor_tensor(w_rest[:, :, :].rearrange("p s m -> p (s m)"), w_sum[:, :],
                                        w_head[:, :, :].rearrange("p s m -> p (s m)").bitcast(F32),
                                        ALU.subtract).then_inc(w_rest_ready, 1)

            def split_rest(n, slot):
                dve.wait_ge(head_ready, n + 1)
                nc.vector.tensor_tensor(split_view(rest, slot), x_view(slot), split_view(head, slot).bitcast(F32),
                                        ALU.subtract).then_inc(rest_ready, 1)

            def copy_odd(n, slot, new_kernel_of=None):
                to, of = upper_of_odd(head, slot)
                nc.vector.tensor_copy(to, of).then_inc(odd_head_up_ready, 1)
                dve.wait_ge(rest_ready, n + 1)
                to, of = lower_of_odd(rest, slot)
                nc.vector.tensor_copy(to, of).then_inc(odd_rest_ready, 1)
                if new_kernel_of is not None:
                    split_w_rest(new_kernel_of)
                to, of = upper_of_odd(rest, slot)
                nc.vector.tensor_copy(to, of).then_inc(odd_rest_ready, 1)

            def pair_stats(n, t, half, slot):
                dve.wait_ge(raw_copied, PAIRS * n + half + 1)
                for a in range(2):
                    last = nc.vector.bn_stats(stats[:, bass.ds(4 * t + 2 * half + a, 1), :].rearrange("p o s -> p (o s)"),
                                              raw_tile[:, slot, 4 * half + 2 * a:4 * half + 2 * a + 2, :]
                                              .rearrange("p w c -> p (w c)"))
                last.then_inc(stats_done, 1)

            def tile_stats(n, t, slot):
                for half in range(PAIRS):
                    pair_stats(n, t, half, slot)

            def aggregate(b):
                dve.wait_ge(stats_done, PAIRS * TILES * (b + 1))
                nc.vector.memset(count[:, :], float(H * W // G))
                nc.vector.bn_aggr(sample_mv[:, :], stats[:, :, :].rearrange("p c s -> p (c s)")).then_inc(aggr_done, 1)
                dve.wait_ge(aggr_done, 3 * b + 1)
                one = triples[:, bass.ds(b, 1), :].rearrange("p o s -> p (o s)")
                nc.vector.tensor_copy(one[:, 1:2], sample_mv[:, 0:1]).then_inc(aggr_done, 1)
                nc.vector.tensor_scalar(one[:, 2:3], sample_mv[:, 1:2], float(H * W // G), None,
                                        ALU.mult).then_inc(aggr_done, 1)
                dve.wait_ge(aggr_done, 3 * b + 3)

            dve.wait_ge(params_loaded, 16 * 4)
            attention(0)
            combine(0)
            split_rest(0, 0)
            split_w_rest(0)
            copy_odd(0, 0)

            def step(b, t, slot):
                n = TILES * b + t
                other = 1 - slot
                last_sample = fixed(b) and b == B - 1
                final = fixed(t) and t == TILES - 1
                makes_kernel = fixed(t) and t == TILES - 2 and not last_sample
                if makes_kernel:
                    attention(b + 1)
                if not (final and last_sample):
                    split_rest(n + 1, other)
                    copy_odd(n + 1, other, b + 1 if final else None)
                if makes_kernel:
                    combine(b + 1)
                if not (fixed(t) and t == 0):
                    tile_stats(n - 1, t - 1, other)
                elif not (fixed(b) and b == 0):
                    tile_stats(n - 1, TILES - 1, other)
                    aggregate(b - 1)

            all_samples(dve, lambda b, i: tiles_of_sample(dve, b, step))
            tile_stats(B * TILES - 1, TILES - 1, 1)
            aggregate(B - 1)

            chain = [0]

            def link(ins):
                chain[0] += 1
                ins.then_inc(fin_chain, 1)
                dve.wait_ge(fin_chain, chain[0])

            nc.vector.bn_aggr(total[:, :], triples[:, :, :].rearrange("p b s -> p (b s)")).then_inc(mean_ready, 1)
            dve.wait_ge(meansum_ready, 1)
            link(nc.vector.tensor_copy(own[:, 0:1], ps[:, 0, 0:1]))
            link(nc.vector.tensor_tensor(own[:, 1:2], total[:, 0:1], own[:, 0:1], ALU.subtract))
            link(nc.vector.tensor_tensor(own[:, 2:3], own[:, 1:2], own[:, 1:2], ALU.mult))
            link(nc.vector.tensor_tensor(own[:, 3:4], own[:, 2:3], total[:, 1:2], ALU.add))
            quarter = same_channel[:, :, 0]
            link(nc.vector.tensor_scalar(by_channel[:, 3, :], quarter, own[:, 3:4], None, ALU.mult))
            nc.vector.tensor_scalar(by_channel[:, 4, :], quarter, total[:, 0:1], None, ALU.mult).then_inc(dev_ready, 1)
            dve.wait_ge(var_ready, 1)
            nc.vector.tensor_scalar(by_channel[:, 1, :], ps[:, 1, 0:CO], EPS, None, ALU.add).then_inc(varsum_ready, 1)
            link(nc.vector.tensor_copy(by_channel[:, 0, :], ps[:, 1, CO:2 * CO]))
            dve.wait_ge(sqrt_ready, 1)
            mean, var, root, rstd, square, product, factor, sharp = (by_channel[:, i, :] for i in range(8))
            link(nc.vector.reciprocal(rstd, root))
            link(nc.vector.tensor_tensor(square, rstd, rstd, ALU.mult))
            link(nc.vector.tensor_tensor(product, square, var, ALU.mult))
            link(nc.vector.tensor_scalar(factor, product, -0.5, 1.5, ALU.mult, ALU.add))
            link(nc.vector.tensor_tensor(sharp, factor, rstd, ALU.mult))
            link(nc.vector.tensor_tensor(scale[:, :], sharp, gam[:, :], ALU.mult))
            link(nc.vector.tensor_tensor(square, scale[:, :], mean, ALU.mult))
            nc.vector.tensor_tensor(shift[:, :], bet[:, :], square, ALU.subtract).then_inc(scale_ready, 1)

        @block.tensor
        def _(pe):
            pe.wait_ge(k_rows_set, 3)
            pe.wait_ge(consts_set, 3)
            for ro in range(2):
                for dx in range(KS):
                    i = ro * KS + dx
                    rows = k_rows[:, ro, dx, :, :].rearrange("p g i -> p (g i)")
                    last = nc.tensor.matmul(ps[:, i // 4, (i % 4) * P:(i % 4 + 1) * P], rows, ident[:, :],
                                            start=True, stop=True)
            last.then_inc(taps_turned, 1)

            def total_pool(b):
                pe.wait_ge(pool_summed, CI * (b + 1))
                nc.tensor.matmul(ps[:, 3, 0:CI], ones[:, :], sums[:, :], start=True, stop=True).then_inc(pool_total, 1)

            total_pool(0)

            def step(b, t, slot):
                n = TILES * b + t
                if not fixed(n) or n >= 2:
                    pe.wait_ge(raw_copied, PAIRS * n - 2)
                if fixed(t) and t == 0:
                    pe.wait_ge(w_head_ready, b + 1)
                pools = fixed(t) and t == TILES - 2 and not (fixed(b) and b == B - 1)
                pe.wait_ge(odd_head_low_ready, n + 1)
                pe.wait_ge(odd_head_up_ready, n + 1)
                for bank in range(4):
                    if bank == 1 and pools:
                        total_pool(b + 1)
                    if bank == 3 and pools:
                        pe.wait_ge(pool_total_read, b + 2)
                    products = ((w_head, head), (w_rest, head), (w_head, rest))
                    if bank > 0:
                        products = ((w_head, head), (w_head, rest), (w_rest, head))
                    for i, (w, part) in enumerate(products):
                        if i == 1 and bank == 0 and fixed(t) and t == 0:
                            pe.wait_ge(w_rest_ready, b + 1)
                        if i == 2 and bank == 0:
                            pe.wait_ge(odd_rest_ready, 2 * n + 2)
                        for s in range(TAPS):
                            at = (ODD - 1, 0, ODD, 1)[s]
                            last = nc.tensor.matmul(ps[:, 4 * slot + bank, :], w[:, s, :],
                                                    part[:, slot, 2 * bank:2 * bank + 2, at:at + X],
                                                    start=(i == 0 and s == 0), stop=(i == 2 and s == TAPS - 1))
                        if i == 1 and bank == 3 and fixed(t) and t == TILES - 1:
                            last.then_inc(w_head_used, 1)
                    if bank % 2:
                        last.then_inc(pair_done, 1)

            all_samples(pe, lambda b, i: tiles_of_sample(pe, b, step))

            pe.wait_ge(same_channel_set, 1 + G)
            pe.wait_ge(mean_ready, 1)
            pe.wait_ge(raw_copied, PAIRS * B * TILES)
            sel = same_channel[:, :, :].rearrange("p c g -> p (c g)")
            nc.tensor.matmul(ps[:, 0, 0:1], sel, total[:, 0:1], start=True, stop=True).then_inc(meansum_ready, 1)
            pe.wait_ge(dev_ready, 1)
            nc.tensor.matmul(ps[:, 1, 0:2 * CO], ones[:, :], by_channel[:, 3:5, :], start=True,
                             stop=True).then_inc(var_ready, 1)


_INS = ['x', 'L0_conv_kernels', 'L0_conv_w_att', 'L0_conv_b_att', 'L0_conv_gamma', 'L0_conv_beta']


def kernel(**inputs):
    import numpy as _np
    import concourse.bacc as _bacc
    from concourse import mybir as _mybir
    from concourse.bass_utils import run_bass_kernel_spmd as _run

    nc = _bacc.Bacc("TRN2", target_bir_lowering=False, num_devices=1)
    arrays, args = {}, []
    for name in _INS:
        a = _np.ascontiguousarray(inputs[name])
        arrays[f"in_{name}_dram"] = a
        args.append(nc.dram_tensor(f"in_{name}_dram", a.shape, _mybir.dt.from_np(a.dtype), kind="ExternalInput").ap())
    shape = inputs['x'].shape[:1] + (inputs['L0_conv_kernels'].shape[1],) + inputs['x'].shape[2:]
    args.append(nc.dram_tensor("out_dram", shape, _mybir.dt.float32, kind="ExternalOutput").ap())
    dynamic_conv_batchnorm_relu(nc, *args)
    r = _run(nc, [arrays], core_ids=[0])
    return r.results[0]["out_dram"]
```
